# Optimizing a Trainium2 kernel written in Bass

```python
import numpy as np
import jax
import jax.numpy as jnp

def _softmax(x, axis=-1):
    return jax.nn.softmax(x, axis=axis)

def _gelu(x):
    return jax.nn.gelu(x, approximate=True)

def _silu(x):
    return jax.nn.silu(x)

def _sigmoid(x):
    return jax.nn.sigmoid(x)

def _layernorm(x, axis=-1, eps=1e-05):
    m = jnp.mean(x, axis=axis, keepdims=True)
    v = jnp.var(x, axis=axis, keepdims=True)
    return (x - m) / jnp.sqrt(v + eps)

def _scatter_add(tgt, idx, src, axis=0):
    return tgt.at[idx].add(src)

def _segment_sum(src, seg, n):
    return jax.ops.segment_sum(src, seg, n)
kernel_name = 'mk_cond_resid_d1_seqx_r4_2056f0'

def setup_inputs(seed: int=0):
    np.random.seed(seed)
    _w = jnp.asarray

    def _rec_inputs():
        import jax
        import jax.numpy as jnp
        _rk = jax.random.key(seed)
        x = -0.000125 + 0.9999 * jax.random.normal(jax.random.fold_in(_rk, 1), (32, 256, 256), jnp.float32)
        _lenS = 256 - jax.random.randint(jax.random.fold_in(_rk, 7), (32,), 0, max(1, 256 // 4) + 1, jnp.int32)
        _lenS2 = 256 - jax.random.randint(jax.random.fold_in(_rk, 8), (32,), 0, max(1, 256 // 4) + 1, jnp.int32)
        itok_B_0_15 = jax.random.randint(jax.random.fold_in(_rk, 11), (32,), 0, 16, jnp.int32)
        return (x, itok_B_0_15)
    x, itok_B_0_15 = _rec_inputs()

    def _L0_cond_setup():
        import jax, jax.numpy as jnp
        import numpy as np
        B, N, DIM = (32, 256, 256)
        HID = 1024
        PART = 64
        OUT = 256
        SHARED = OUT - PART
        E = 16
        key = jax.random.key(seed)
        ks = jax.random.split(key, 8)
        s = 0.02
        return {'x': jax.random.normal(ks[0], (B, N, DIM), dtype=jnp.float32), 'indices': jax.random.randint(ks[1], (B,), 0, E, dtype=jnp.int64), 'fc1_w': jax.random.normal(ks[2], (HID, DIM), dtype=jnp.float32) * s, 'fc1_b': jnp.zeros((HID,), dtype=jnp.float32), 'fc2_w': jax.random.normal(ks[3], (SHARED, HID), dtype=jnp.float32) * s, 'fc2_b': jnp.zeros((SHARED,), dtype=jnp.float32), 'experts_w': jax.random.normal(ks[4], (E, PART, HID), dtype=jnp.float32) * s, 'experts_b': jnp.zeros((E, PART), dtype=jnp.float32)}
    _L0_cond_all = _L0_cond_setup()
    _L0_cond_in = {k: v for k, v in _L0_cond_all.items() if k in ('fc1_w', 'fc1_b', 'fc2_w', 'fc2_b', 'experts_w', 'experts_b')}
    del _L0_cond_all
    return {'x': x, 'itok_B_0_15': itok_B_0_15, 'L0_cond_fc1_w': _L0_cond_in['fc1_w'], 'L0_cond_fc1_b': _L0_cond_in['fc1_b'], 'L0_cond_fc2_w': _L0_cond_in['fc2_w'], 'L0_cond_fc2_b': _L0_cond_in['fc2_b'], 'L0_cond_experts_w': _L0_cond_in['experts_w'], 'L0_cond_experts_b': _L0_cond_in['experts_b']}

def reference(x, itok_B_0_15, L0_cond_fc1_w, L0_cond_fc1_b, L0_cond_fc2_w, L0_cond_fc2_b, L0_cond_experts_w, L0_cond_experts_b):
    import jax
    import jax.numpy as jnp

    def _L0_cond_ref(x, indices, fc1_w, fc1_b, fc2_w, fc2_b, experts_w, experts_b):
        import jax, jax.numpy as jnp
        import numpy as np
        B, N, DIM = (32, 256, 256)
        HID = 1024
        PART = 64
        OUT = 256
        SHARED = OUT - PART
        E = 16
        h = jax.nn.gelu(jnp.einsum('bnd,hd->bnh', x, fc1_w) + fc1_b, approximate=False)
        shared = jnp.einsum('bnh,sh->bns', h, fc2_w) + fc2_b
        We = experts_w[indices]
        be = experts_b[indices]
        expert_x = jnp.einsum('bnh,bph->bnp', h, We) + be[:, None, :]
        return jnp.concatenate([shared, expert_x], axis=-1)
    x = x + _L0_cond_ref(x, itok_B_0_15, L0_cond_fc1_w, L0_cond_fc1_b, L0_cond_fc2_w, L0_cond_fc2_b, L0_cond_experts_w, L0_cond_experts_b)
    return x

_drawn_inputs = setup_inputs


def setup_inputs(seed=0):
    import zlib

    import numpy as np

    out = dict(_drawn_inputs(seed))
    spreads = {'L0_cond_fc1_b': (0.0, 0.1), 'L0_cond_fc2_b': (0.0, 0.1), 'L0_cond_experts_b': (0.0, 0.1)}
    factors = {}
    for name, (base, spread) in spreads.items():
        noise = np.random.default_rng([zlib.crc32(name.encode()), seed]).standard_normal(out[name].shape)
        drawn = base * np.exp(spread * noise) if base else spread * noise
        out[name] = jnp.asarray(drawn.astype(out[name].dtype))
    for name, factor in factors.items():
        out[name] = (out[name] * factor).astype(out[name].dtype)
    return out
```

```python
from contextlib import ExitStack

import concourse.bass as bass
from concourse import mybir

FP32 = mybir.dt.float32
FP32R = mybir.dt.float32r
ALU = mybir.AluOpType
ACT = mybir.ActivationFunctionType

HI, LO = 0, 1


def cond_mlp_residual(nc, x, index, fc1_w, fc1_b, fc2_w, fc2_b, experts_w, experts_b, out):
    P = 128
    ROWS, SEQ, DIM = x.shape
    HID = fc1_w.shape[0]
    SHARED = fc2_w.shape[0]
    E, PART = experts_w.shape[0], experts_w.shape[1]
    OUT = SHARED + PART
    B = 2
    T = SEQ // P
    TILES = B * T
    TOK = TILES * P
    BLOCKS = ROWS // B
    D = DIM // P
    K = HID // P
    HALF = K // 2
    BANK = 512
    FC1_BANKS = 4

    x_blocks = x.rearrange("(n b) (p t) d -> n p b (t d)", b=B, t=T)
    out_blocks = out.rearrange("(n b) (p t) d -> n p b (t d)", b=B, t=T)

    ctx = ExitStack()
    with ctx:
        def sbuf(name, shape, dtype=FP32):
            return ctx.enter_context(nc.sbuf_tensor(name, shape, dtype))

        def psum(name, shape):
            return ctx.enter_context(nc.psum_tensor(name, shape, FP32))

        def sem(name):
            return ctx.enter_context(nc.semaphore(name))

        w1t = sbuf("w1t", [P, D, 2, HID], FP32R)
        w2t = sbuf("w2t", [P, 2, B, K, 2 * OUT], FP32R)
        xt = sbuf("xt", [P, 2, D, 2, TOK], FP32R)
        ht = sbuf("ht", [P, 2, 2, K, TOK], FP32R)
        gelu = sbuf("gelu", [P, 2, 2 * TOK])
        x_in = sbuf("x_in", [P, 2, B, T * DIM])
        resid = sbuf("resid", [P, 2, B, T * DIM])
        e_in = sbuf("e_in", [P, 2, HID])
        w2_in = sbuf("w2_in", [P, 2, HID])
        bias = sbuf("bias", [P, 2, B, OUT])
        ident = sbuf("ident", [P, P])
        b1_in = sbuf("b1_in", [K, P])
        b1 = sbuf("b1", [P, K])
        index_sb = sbuf("index_sb", [1, ROWS], mybir.dt.int32)
        w1_in = resid[:, :, :, :].rearrange("p a b (t d) -> p (a b t) d", d=DIM)

        fc1_ps = psum("fc1_ps", [P, FC1_BANKS, BANK])
        acc_ps = psum("acc_ps", [P, 2, BANK])
        tr_ps = psum("tr_ps", [P, 2, BANK])

        w1_loaded = [sem(f"w1_loaded{n}") for n in range(2)]
        w2_loaded = sem("w2_loaded")
        b1_loaded = sem("b1_loaded")
        b2_loaded = sem("b2_loaded")
        index_loaded = sem("index_loaded")
        x_loaded = [sem(f"x_loaded{n}") for n in range(2)]
        e_loaded = [sem(f"e_loaded{n}") for n in range(2)]
        be_loaded = [sem(f"be_loaded{n}") for n in range(2)]
        stored = [sem(f"stored{n}") for n in range(2)]
        ident_zeroed = sem("ident_zeroed")
        ident_ready = sem("ident_ready")
        tr_filled = sem("tr_filled")
        tr_hi = sem("tr_hi")
        tr_lo = sem("tr_lo")
        acc_filled = sem("acc_filled")
        acc_hi = sem("acc_hi")
        acc_drained = sem("acc_drained")
        fc1_filled = sem("fc1_filled")
        gelu_done = sem("gelu_done")
        h_hi = sem("h_hi")
        h_lo = sem("h_lo")
        w2_copied = sem("w2_copied")
        resid_ready = sem("resid_ready")
        cross_added = sem("cross_added")

        TR_W1 = {(0, 0): 0, (0, 1): 1, (1, 0): 4, (1, 1): 5}
        TR_X0, TR_E0, TR_X1, TR_FIRST = 2, 6, 8, 10
        ACC_FIRST = 1 + K // 2
        PAIRS = (BLOCKS - 4) // 2

        block = ctx.enter_context(nc.Block())

        @block.sync
        def _(sp):
            def expert_numbers(row):
                return [sp.value_load(index_sb[0:1, bass.ds(row + b, 1)], min_val=0, max_val=E - 1)
                        for b in range(B)]

            def load_experts(par, experts):
                for b, e in enumerate(experts):
                    sp.dma_start(e_in[b * PART:(b + 1) * PART, par, :],
                                 experts_w[bass.ds(e, 1), :, :].rearrange("o p h -> (o p) h"))\
                        .then_inc(e_loaded[par], 16)
                    sp.dma_start(bias[:, par, b, SHARED:OUT],
                                 experts_b[bass.ds(e, 1), :].to_broadcast([P, PART]))\
                        .then_inc(be_loaded[par], 16)

            def load_x(i, par):
                sp.dma_start(x_in[:, par, :, :], x_blocks[i]).then_inc(x_loaded[par], 16)

            def step(i, par, x_ahead=True, e_ahead=True):
                nxt = 1 - par
                if e_ahead:
                    experts = expert_numbers(B * (i + 2))
                    sp.wait_ge(tr_filled, TR_FIRST + 4 * i - 2)
                    load_experts(par, experts)
                if x_ahead:
                    sp.wait_ge(tr_filled, TR_FIRST + 4 * i)
                    sp.wait_ge(resid_ready, i + 2)
                    load_x(i + 3, nxt)
                for b in range(B):
                    sp.wait_ge(acc_drained, ACC_FIRST + TILES * i + T * (b + 1))
                    sp.dma_start(out_blocks[i][:, b, :], resid[:, par, b, :])\
                        .then_inc(stored[par], 16)

            w1_v = fc1_w.rearrange("(c p) d -> p c d", p=P)
            sp.dma_start(w1_in[:, 0:HALF, :], w1_v[:, 0:HALF, :]).then_inc(w1_loaded[0], 16)
            sp.dma_start(w1_in[:, HALF:K, :], w1_v[:, HALF:K, :]).then_inc(w1_loaded[1], 16)
            sp.dma_start(w2_in[:, 0, :], fc2_w[0:P, :]).then_inc(w2_loaded, 16)
            sp.dma_start(w2_in[0:SHARED - P, 1, :], fc2_w[P:SHARED, :]).then_inc(w2_loaded, 16)
            sp.wait_ge(index_loaded, 16)
            load_experts(0, expert_numbers(0))
            load_x(1, 1)
            load_experts(1, expert_numbers(B))
            sp.wait_ge(tr_filled, TR_X0 + 2)
            sp.wait_ge(resid_ready, 1)
            load_x(2, 0)

            step(0, 0)
            with sp.Fori(0, PAIRS) as m:
                step(2 * m + 1, 1)
                step(2 * m + 2, 0)
            step(BLOCKS - 3, 1, x_ahead=False)
            step(BLOCKS - 2, 0, x_ahead=False, e_ahead=False)
            step(BLOCKS - 1, 1, x_ahead=False, e_ahead=False)
            for par in range(2):
                sp.wait_ge(stored[par], 16 * B * BLOCKS // 2)

        @block.gpsimd
        def _(pool):
            def residual(i, par, use):
                pool.wait_ge(x_loaded[par], 16 * (use + 1))
                pool.wait_ge(be_loaded[par], 16 * B * (use + 1))
                pool.wait_ge(stored[par], 16 * B * use)
                nc.gpsimd.tensor_tensor(
                    resid[:, par, :, :].rearrange("p b (t d) -> p b t d", t=T),
                    x_in[:, par, :, :].rearrange("p b (t d) -> p b t d", t=T),
                    bias[:, par, :, :].unsqueeze(2).to_broadcast([P, B, T, OUT]),
                    ALU.add).then_inc(resid_ready, 1)

            nc.gpsimd.memset(ident[:, :], 0.0).then_inc(ident_zeroed, 1)
            pool.wait_ge(ident_zeroed, 1)
            nc.gpsimd.affine_select(out=ident[:, :], in_=ident[:, :], compare_op=ALU.not_equal,
                                    fill=1.0, base=0, pattern=[[-1, P]], channel_multiplier=1)\
                .then_inc(ident_ready, 1)
            pool.wait_ge(tr_filled, TR_W1[1, 1] + 1)
            pool.wait_ge(b2_loaded, 16 * 2 * B)
            residual(0, 0, 0)
            pool.wait_ge(acc_drained, ACC_FIRST)
            for par, b in ((0, 1), (1, 0), (1, 1)):
                for part in (HI, LO):
                    cols = slice(part * OUT, part * OUT + SHARED)
                    nc.gpsimd.tensor_copy(w2t[:, par, b, :, cols],
                                          w2t[:, 0, 0, :, cols].bitcast(FP32))\
                        .then_inc(w2_copied, 1)
            residual(1, 1, 0)
            with pool.Fori(0, PAIRS) as m:
                residual(2 * m + 2, 0, m + 1)
                residual(2 * m + 3, 1, m + 1)
            residual(BLOCKS - 2, 0, BLOCKS // 2 - 1)
            residual(BLOCKS - 1, 1, BLOCKS // 2 - 1)

        @block.scalar
        def _(act):
            def transposed_hi(dst, src, n):
                act.wait_ge(tr_filled, n + 1)
                nc.scalar.activation(dst, src, ACT.Copy).then_inc(tr_hi, 1)

            def experts_hi(par, n, half, bank):
                transposed_hi(
                    w2t[:, par, :, half * HALF:(half + 1) * HALF, SHARED:OUT],
                    tr_ps[:, bank, :].rearrange("p (k b c) -> p b k c", k=HALF, b=B), n)

            def x_hi(par, n, d, bank):
                transposed_hi(xt[:, par, d, HI, :], tr_ps[:, bank, :], n)

            def w1_hi(half, d):
                n = TR_W1[half, d]
                transposed_hi(w1t[:, d, HI, half * HALF * P:(half + 1) * HALF * P],
                              tr_ps[:, n % 2, :], n)

            def shared_hi(f):
                act.wait_ge(acc_filled, f + 1)
                k = 2 * (f - 1)
                nc.scalar.activation(
                    w2t[:, 0, 0, k:k + 2, 0:SHARED],
                    acc_ps[:, f % 2, :].rearrange("p (k c) -> p k c", k=2)[:, :, 0:SHARED],
                    ACT.Copy).then_inc(acc_hi, 1)

            def chunk(i, par, j):
                n = K * i + j
                r = j // 2
                act.wait_ge(fc1_filled, n + 1)
                if j % 2 == 0 and not (isinstance(i, int) and i == 0 and r < 2):
                    act.wait_ge(h_lo, HALF * i + r - 1)
                half = slice((j % 2) * TOK, (j % 2 + 1) * TOK)
                nc.scalar.activation(gelu[:, r % 2, half], fc1_ps[:, j % FC1_BANKS, :],
                                     ACT.Gelu, bias=b1[:, j:j + 1]).then_inc(gelu_done, 1)
                if j % 2 == 1:
                    act.wait_ge(gelu_done, n + 1)
                    nc.scalar.activation(
                        ht[:, par, HI, 2 * r:2 * r + 2, :].rearrange("p k t -> p (k t)"),
                        gelu[:, r % 2, :], ACT.Copy).then_inc(h_hi, 1)

            def step(i, par, x_ahead=True):
                first = TR_FIRST + 4 * i
                for j in range(K):
                    if j in (0, 2):
                        experts_hi(1 - par, first + j // 2, j // 2, j // 2)
                    if j in (4, 6) and x_ahead:
                        x_hi(par, first + j // 2, j // 2 - 2, j // 2 - 2)
                    chunk(i + 1, 1 - par, j)

            act.dma_start(index_sb[:, :], index.rearrange("(o n) -> o n", o=1))\
                .then_inc(index_loaded, 16)
            act.dma_start(x_in[:, 0, :, :], x_blocks[0]).then_inc(x_loaded[0], 16)
            act.dma_start(b1_in[:, :], fc1_b.rearrange("(k p) -> k p", p=P))\
                .then_inc(b1_loaded, 16)
            for par in range(2):
                for b in range(B):
                    act.dma_start(bias[:, par, b, 0:SHARED],
                                  fc2_b.rearrange("(o n) -> o n", o=1).to_broadcast([P, SHARED]))\
                        .then_inc(b2_loaded, 16)
            w1_hi(0, 0)
            w1_hi(0, 1)
            for d in range(D):
                x_hi(0, TR_X0 + d, d, d)
            act.wait_ge(acc_drained, 1)
            for j in range(K):
                if j == 1:
                    w1_hi(1, 0)
                    w1_hi(1, 1)
                if j in (3, 4, 5, 6):
                    shared_hi(j - 2)
                if j == 6:
                    experts_hi(0, TR_E0, 0, 0)
                if j == 7:
                    experts_hi(0, TR_E0 + 1, 1, 1)
                chunk(0, 0, j)
            for d in range(D):
                x_hi(1, TR_X1 + d, d, d)

            step(0, 0)
            with act.Fori(0, PAIRS) as m:
                step(2 * m + 1, 1)
                step(2 * m + 2, 0)
            step(BLOCKS - 3, 1)
            step(BLOCKS - 2, 0, x_ahead=False)

        @block.vector
        def _(dve):
            def transposed_lo(dst, src, hi, n):
                dve.wait_ge(tr_hi, n + 1)
                nc.vector.tensor_tensor(dst, src, hi.bitcast(FP32), ALU.subtract)\
                    .then_inc(tr_lo, 1)

            def experts_lo(par, n, half, bank):
                ks = slice(half * HALF, (half + 1) * HALF)
                transposed_lo(
                    w2t[:, par, :, ks, OUT + SHARED:2 * OUT],
                    tr_ps[:, bank, :].rearrange("p (k b c) -> p b k c", k=HALF, b=B),
                    w2t[:, par, :, ks, SHARED:OUT], n)

            def x_lo(par, n, d, bank):
                transposed_lo(xt[:, par, d, LO, :], tr_ps[:, bank, :], xt[:, par, d, HI, :], n)

            def w1_lo(half, d):
                n = TR_W1[half, d]
                cols = slice(half * HALF * P, (half + 1) * HALF * P)
                transposed_lo(w1t[:, d, LO, cols], tr_ps[:, n % 2, :], w1t[:, d, HI, cols], n)

            def shared_lo(f):
                dve.wait_ge(acc_hi, f)
                k = 2 * (f - 1)
                nc.vector.tensor_tensor(
                    w2t[:, 0, 0, k:k + 2, OUT:OUT + SHARED],
                    acc_ps[:, f % 2, :].rearrange("p (k c) -> p k c", k=2)[:, :, 0:SHARED],
                    w2t[:, 0, 0, k:k + 2, 0:SHARED].bitcast(FP32), ALU.subtract)\
                    .then_inc(acc_drained, 1)

            def pair_lo(i, par, r):
                dve.wait_ge(h_hi, HALF * i + r + 1)
                nc.vector.tensor_tensor(
                    ht[:, par, LO, 2 * r:2 * r + 2, :].rearrange("p k t -> p (k t)"),
                    gelu[:, r % 2, :],
                    ht[:, par, HI, 2 * r:2 * r + 2, :].rearrange("p k t -> p (k t)").bitcast(FP32),
                    ALU.subtract).then_inc(h_lo, 1)

            def tile_out(i, par, t):
                q = TILES * i + t
                bank = (ACC_FIRST + t) % 2
                dst = resid[:, par, t // T, (t % T) * DIM:(t % T + 1) * DIM]
                dve.wait_ge(acc_filled, ACC_FIRST + q + 1)
                if t == 0:
                    dve.wait_ge(resid_ready, i + 1)
                nc.vector.tensor_tensor(dst, acc_ps[:, bank, OUT:2 * OUT], dst, ALU.add)\
                    .then_inc(cross_added, 1)
                dve.wait_ge(cross_added, q + 1)
                nc.vector.tensor_tensor(dst, acc_ps[:, bank, 0:OUT], dst, ALU.add)\
                    .then_inc(acc_drained, 1)

            def step(i, par, x_ahead=True):
                first = TR_FIRST + 4 * i
                for j in range(K):
                    if j in (0, 2):
                        experts_lo(1 - par, first + j // 2, j // 2, j // 2)
                    if j in (4, 6) and x_ahead:
                        x_lo(par, first + j // 2, j // 2 - 2, j // 2 - 2)
                    if j % 2 == 1:
                        pair_lo(i + 1, 1 - par, j // 2)
                        tile_out(i, par, j // 2)

            w1_lo(0, 0)
            w1_lo(0, 1)
            for d in range(D):
                x_lo(0, TR_X0 + d, d, d)
            dve.wait_ge(acc_filled, 1)
            nc.vector.tensor_copy(b1[:, :], acc_ps[:, 0, 0:K]).then_inc(acc_drained, 1)
            for j in range(K):
                if j == 1:
                    w1_lo(1, 0)
                    w1_lo(1, 1)
                if j in (3, 4, 5, 6):
                    shared_lo(j - 2)
                if j == 6:
                    experts_lo(0, TR_E0, 0, 0)
                if j == 7:
                    experts_lo(0, TR_E0 + 1, 1, 1)
                if j % 2 == 1:
                    pair_lo(0, 0, j // 2)
            for d in range(D):
                x_lo(1, TR_X1 + d, d, d)

            step(0, 0)
            with dve.Fori(0, PAIRS) as m:
                step(2 * m + 1, 1)
                step(2 * m + 2, 0)
            step(BLOCKS - 3, 1)
            step(BLOCKS - 2, 0, x_ahead=False)
            for t in range(TILES):
                tile_out(BLOCKS - 1, 1, t)

        @block.tensor
        def _(pe):
            def transpose_bank(n, bank, pieces):
                if not (isinstance(n, int) and n < 2):
                    pe.wait_ge(tr_lo, n - 1)
                for c, piece in enumerate(pieces):
                    last = nc.tensor.transpose(tr_ps[:, bank, c * P:(c + 1) * P], piece,
                                               ident[:, :])
                last.then_inc(tr_filled, 1)

            def w1_bank(half, d):
                n = TR_W1[half, d]
                pe.wait_ge(w1_loaded[half], 16)
                transpose_bank(n, n % 2, [w1_in[:, c, d * P:(d + 1) * P]
                                          for c in range(half * HALF, (half + 1) * HALF)])

            def x_bank(par, use, n, d, bank):
                if d == 0:
                    pe.wait_ge(x_loaded[par], 16 * (use + 1))
                transpose_bank(n, bank, [
                    x_in[:, par, t // T, (t % T) * DIM + d * P:(t % T) * DIM + (d + 1) * P]
                    for t in range(TILES)])

            def experts_bank(par, use, n, half, bank):
                if half == 0:
                    pe.wait_ge(e_loaded[par], 16 * B * (use + 1))
                transpose_bank(n, bank, [e_in[:, par, k * P:(k + 1) * P]
                                         for k in range(half * HALF, (half + 1) * HALF)])

            def shared_bank(f):
                if f == 1:
                    pe.wait_ge(w2_loaded, 32)
                else:
                    pe.wait_ge(acc_drained, f - 1)
                for c in range(2):
                    k = 2 * (f - 1) + c
                    ks = slice(k * P, (k + 1) * P)
                    at = c * (BANK // 2)
                    nc.tensor.transpose(acc_ps[:, f % 2, at:at + P], w2_in[:, 0, ks], ident[:, :])
                    last = nc.tensor.transpose(acc_ps[:, f % 2, at + P:at + SHARED],
                                               w2_in[0:SHARED - P, 1, ks],
                                               ident[0:SHARED - P, 0:SHARED - P])
                last.then_inc(acc_filled, 1)

            def stage2_chunk(i, par, j):
                n = K * i + j
                if not (isinstance(i, int) and i == 0 and j < FC1_BANKS):
                    pe.wait_ge(gelu_done, n - FC1_BANKS + 1)
                js = slice(j * P, (j + 1) * P)
                terms = [(d, w, v) for d in range(D) for w, v in ((HI, HI), (HI, LO), (LO, HI))]
                for at, (d, w, v) in enumerate(terms):
                    last = nc.tensor.matmul(fc1_ps[:, j % FC1_BANKS, :], w1t[:, d, w, js],
                                            xt[:, par, d, v, :],
                                            start=(at == 0), stop=(at == len(terms) - 1))
                last.then_inc(fc1_filled, 1)

            def stage3_half(i, par, t, half):
                q = TILES * i + t
                bank = (ACC_FIRST + t) % 2
                if half == 0:
                    pe.wait_ge(acc_drained, ACC_FIRST + q - 1)
                if t == 0:
                    pe.wait_ge(h_lo, HALF * i + (half + 1) * HALF // 2)
                ts = slice(t * P, (t + 1) * P)
                for k in range(half * HALF, (half + 1) * HALF):
                    nc.tensor.matmul(acc_ps[:, bank, :], ht[:, par, HI, k, ts],
                                     w2t[:, par, t // T, k, :], start=(k == 0), stop=False)
                    last = nc.tensor.matmul(acc_ps[:, bank, OUT:2 * OUT], ht[:, par, LO, k, ts],
                                            w2t[:, par, t // T, k, 0:OUT],
                                            start=False, stop=(k == K - 1))
                if half == 1:
                    last.then_inc(acc_filled, 1)

            def step(i, par, e_use, x_use, x_ahead=True):
                first = TR_FIRST + 4 * i
                for j in range(K):
                    if j in (0, 2):
                        experts_bank(1 - par, e_use, first + j // 2, j // 2, j // 2)
                    if j in (4, 6) and x_ahead:
                        x_bank(par, x_use, first + j // 2, j // 2 - 2, j // 2 - 2)
                    if j == 0:
                        pe.wait_ge(tr_lo, first)
                    stage2_chunk(i + 1, 1 - par, j)
                    stage3_half(i, par, j // 2, j % 2)

            pe.wait_ge(ident_ready, 1)
            pe.wait_ge(b1_loaded, 16)
            nc.tensor.transpose(acc_ps[:, 0, 0:K], b1_in[:, :], ident[0:K, 0:K])\
                .then_inc(acc_filled, 1)
            w1_bank(0, 0)
            w1_bank(0, 1)
            for d in range(D):
                x_bank(0, 0, TR_X0 + d, d, d)
            pe.wait_ge(tr_lo, TR_X0 + D)
            for j in range(K):
                if j == 1:
                    w1_bank(1, 0)
                    w1_bank(1, 1)
                if j in (3, 4, 5, 6):
                    shared_bank(j - 2)
                if j == 4:
                    pe.wait_ge(tr_lo, TR_W1[1, 1] + 1)
                if j in (6, 7):
                    experts_bank(0, 0, TR_E0 + j - 6, j - 6, j - 6)
                stage2_chunk(0, 0, j)
            for d in range(D):
                x_bank(1, 0, TR_X1 + d, d, d)

            pe.wait_ge(w2_copied, 6)
            step(0, 0, 0, 1)
            with pe.Fori(0, PAIRS) as m:
                step(2 * m + 1, 1, m + 1, m + 1)
                step(2 * m + 2, 0, m + 1, m + 2)
            step(BLOCKS - 3, 1, BLOCKS // 2 - 1, BLOCKS // 2 - 1)
            step(BLOCKS - 2, 0, BLOCKS // 2 - 1, 0, x_ahead=False)
            for t in range(TILES):
                for half in range(2):
                    stage3_half(BLOCKS - 1, 1, t, half)


_INS = ["x", "itok_B_0_15", "L0_cond_fc1_w", "L0_cond_fc1_b", "L0_cond_fc2_w", "L0_cond_fc2_b",
        "L0_cond_experts_w", "L0_cond_experts_b"]


def kernel(**inputs):
    import numpy as np
    import concourse.bacc as bacc
    from concourse.bass_utils import run_bass_kernel_spmd

    nc = bacc.Bacc("TRN2", target_bir_lowering=False, num_devices=1)
    arrays, args = {}, []
    for name in _INS:
        a = np.ascontiguousarray(inputs[name])
        arrays[f"in_{name}"] = a
        args.append(nc.dram_tensor(f"in_{name}", a.shape, mybir.dt.from_np(a.dtype),
                                   kind="ExternalInput").ap())
    out = nc.dram_tensor("out", arrays["in_x"].shape, FP32, kind="ExternalOutput").ap()
    cond_mlp_residual(nc, *args, out)
    r = run_bass_kernel_spmd(nc, [arrays], core_ids=[0])
    return r.results[0]["out"]
```

```python
from contextlib import ExitStack

import concourse.bass as bass
from concourse import mybir

FP32 = mybir.dt.float32
FP32R = mybir.dt.float32r
ALU = mybir.AluOpType
ACT = mybir.ActivationFunctionType

HI, LO = 0, 1


def cond_mlp_residual(nc, x, index, fc1_w, fc1_b, fc2_w, fc2_b, experts_w, experts_b, out):
    P = 128
    ROWS, SEQ, DIM = x.shape
    HID = fc1_w.shape[0]
    SHARED = fc2_w.shape[0]
    E, PART = experts_w.shape[0], experts_w.shape[1]
    OUT = SHARED + PART
    B = 2
    T = SEQ // P
    TILES = B * T
    TOK = TILES * P
    BLOCKS = ROWS // B
    D = DIM // P
    K = HID // P
    HALF = K // 2
    BANK = 512
    FC1_BANKS = 4
    WARM = 8

    x_blocks = x.rearrange("(n b) (p t) d -> n p b (t d)", b=B, t=T)
    out_blocks = out.rearrange("(n b) (p t) d -> n p b (t d)", b=B, t=T)

    ctx = ExitStack()
    with ctx:
        def sbuf(name, shape, dtype=FP32):
            return ctx.enter_context(nc.sbuf_tensor(name, shape, dtype))

        def psum(name, shape):
            return ctx.enter_context(nc.psum_tensor(name, shape, FP32))

        def sem(name):
            return ctx.enter_context(nc.semaphore(name))

        w1t = sbuf("w1t", [P, D, 2, HID], FP32R)
        w2t = sbuf("w2t", [P, 2, B, K, 2 * OUT], FP32R)
        xt = sbuf("xt", [P, 2, D, 2, TOK], FP32R)
        ht = sbuf("ht", [P, 2, 2, K, TOK], FP32R)
        gelu = sbuf("gelu", [P, 2, 2 * TOK])
        x_in = sbuf("x_in", [P, 2, B, T * DIM])
        resid = sbuf("resid", [P, 2, B, T * DIM])
        e_in = sbuf("e_in", [P, 2, HID])
        w2_in = sbuf("w2_in", [P, 2, HID])
        bias = sbuf("bias", [P, 2, B, OUT])
        ident = sbuf("ident", [P, P])
        b1_in = sbuf("b1_in", [K, P])
        b1 = sbuf("b1", [P, K])
        index_sb = sbuf("index_sb", [1, ROWS], mybir.dt.int32)
        w1_in = resid[:, :, :, :].rearrange("p a b (t d) -> p (a b t) d", d=DIM)

        fc1_ps = psum("fc1_ps", [P, FC1_BANKS, BANK])
        acc_ps = psum("acc_ps", [P, 2, BANK])
        tr_ps = psum("tr_ps", [P, 2, BANK])

        w1_loaded = [sem(f"w1_loaded{n}") for n in range(2)]
        w2_loaded = sem("w2_loaded")
        b1_loaded = sem("b1_loaded")
        b2_loaded = sem("b2_loaded")
        index_loaded = sem("index_loaded")
        x_loaded = [sem(f"x_loaded{n}") for n in range(2)]
        e_loaded = [sem(f"e_loaded{n}") for n in range(2)]
        be_loaded = [sem(f"be_loaded{n}") for n in range(2)]
        stored = [sem(f"stored{n}") for n in range(2)]
        ident_zeroed = sem("ident_zeroed")
        ident_ready = sem("ident_ready")
        tr_filled = sem("tr_filled")
        tr_hi = sem("tr_hi")
        tr_lo = sem("tr_lo")
        acc_filled = sem("acc_filled")
        shared_hi = sem("shared_hi")
        acc_drained = sem("acc_drained")
        fc1_filled = sem("fc1_filled")
        gelu_done = sem("gelu_done")
        h_hi = sem("h_hi")
        h_lo = sem("h_lo")
        row_copied = sem("row_copied")
        odd_copied = sem("odd_copied")
        gelu_loaded = sem("gelu_loaded")
        resid_ready = sem("resid_ready")
        cross_added = sem("cross_added")

        TR_X0, TR_X1, TR_E0, TR_FIRST = 0, 6, 8, 10
        TR_W1 = {(0, 0): 2, (0, 1): 3, (1, 0): 4, (1, 1): 5}

        def w1_transposed(half, d):
            n = TR_W1[half, d]
            return fc1_ps[:, n, :] if half == 0 else tr_ps[:, n % 2, :]

        ACC_FIRST = 1 + K // 2
        PAIRS = (BLOCKS - 4) // 2

        block = ctx.enter_context(nc.Block())

        @block.sync
        def _(sp):
            def expert_numbers(row):
                return [sp.value_load(index_sb[0:1, bass.ds(row + b, 1)], min_val=0, max_val=E - 1)
                        for b in range(B)]

            def load_experts(par, experts):
                for b, e in enumerate(experts):
                    sp.dma_start(e_in[b * PART:(b + 1) * PART, par, :],
                                 experts_w[bass.ds(e, 1), :, :].rearrange("o p h -> (o p) h"))\
                        .then_inc(e_loaded[par], 16)
                    sp.dma_start(bias[:, par, b, SHARED:OUT],
                                 experts_b[bass.ds(e, 1), :].to_broadcast([P, PART]))\
                        .then_inc(be_loaded[par], 16)

            def load_x(i, par):
                sp.dma_start(x_in[:, par, :, :], x_blocks[i]).then_inc(x_loaded[par], 16)

            def step(i, par, x_ahead=True, e_ahead=True):
                nxt = 1 - par
                if e_ahead:
                    experts = expert_numbers(B * (i + 2))
                    sp.wait_ge(tr_filled, TR_E0 + 2 if isinstance(i, int) and i == 0
                               else TR_FIRST + 4 * i - 2)
                    load_experts(par, experts)
                if x_ahead:
                    sp.wait_ge(tr_filled, TR_FIRST + 4 * i)
                    sp.wait_ge(resid_ready, i + 2)
                    load_x(i + 3, nxt)
                for b in range(B):
                    sp.wait_ge(acc_drained, ACC_FIRST + TILES * i + T * (b + 1))
                    sp.dma_start(out_blocks[i][:, b, :], resid[:, par, b, :])\
                        .then_inc(stored[par], 16)

            w1_v = fc1_w.rearrange("(c p) d -> p c d", p=P)
            sp.dma_start(x_in[:, 0, :, :], x_blocks[0]).then_inc(x_loaded[0], 16)
            sp.dma_start(w1_in[:, 0:HALF, :], w1_v[:, 0:HALF, :]).then_inc(w1_loaded[0], 16)
            sp.dma_start(w1_in[:, HALF:K, :], w1_v[:, HALF:K, :]).then_inc(w1_loaded[1], 16)
            sp.dma_start(w2_in[:, 0, :], fc2_w[0:P, :]).then_inc(w2_loaded, 16)
            sp.dma_start(w2_in[0:SHARED - P, 1, :], fc2_w[P:SHARED, :]).then_inc(w2_loaded, 16)
            sp.wait_ge(index_loaded, 16)
            load_x(1, 1)
            load_experts(0, expert_numbers(0))
            load_experts(1, expert_numbers(B))
            sp.wait_ge(tr_filled, TR_X0 + 2)
            sp.wait_ge(resid_ready, 1)
            load_x(2, 0)
            sp.wait_ge(acc_drained, ACC_FIRST)
            for b in range(B):
                for cols in (slice(0, SHARED), slice(OUT, OUT + SHARED)):
                    sp.dma_start(w2t[:, 1, b, :, cols].bitcast(FP32),
                                 w2t[:, 0, 0, :, cols].bitcast(FP32))\
                        .then_inc(odd_copied, 16)

            step(0, 0)
            with sp.Fori(0, PAIRS) as m:
                step(2 * m + 1, 1)
                step(2 * m + 2, 0)
            step(BLOCKS - 3, 1, x_ahead=False)
            step(BLOCKS - 2, 0, x_ahead=False, e_ahead=False)
            for t in range(TILES):
                sp.wait_ge(acc_drained, ACC_FIRST + TILES * (BLOCKS - 1) + t + 1)
                cols = slice((t % T) * DIM, (t % T + 1) * DIM)
                sp.dma_start(out_blocks[BLOCKS - 1][:, t // T, cols], resid[:, 1, t // T, cols])\
                    .then_inc(stored[1], 16)
            sp.wait_ge(stored[0], 16 * B * BLOCKS // 2)
            sp.wait_ge(stored[1], 16 * (B * (BLOCKS // 2 - 1) + TILES))

        @block.gpsimd
        def _(pool):
            def residual(i, par, use):
                pool.wait_ge(x_loaded[par], 16 * (use + 1))
                pool.wait_ge(be_loaded[par], 16 * B * (use + 1))
                pool.wait_ge(stored[par], 16 * B * use)
                nc.gpsimd.tensor_tensor(
                    resid[:, par, :, :].rearrange("p b (t d) -> p b t d", t=T),
                    x_in[:, par, :, :].rearrange("p b (t d) -> p b t d", t=T),
                    bias[:, par, :, :].unsqueeze(2).to_broadcast([P, B, T, OUT]),
                    ALU.add).then_inc(resid_ready, 1)

            nc.gpsimd.memset(ident[:, :], 0.0).then_inc(ident_zeroed, 1)
            pool.wait_ge(ident_zeroed, 1)
            nc.gpsimd.affine_select(out=ident[:, :], in_=ident[:, :], compare_op=ALU.not_equal,
                                    fill=1.0, base=0, pattern=[[-1, P]], channel_multiplier=1)\
                .then_inc(ident_ready, 1)
            pool.dma_start(
                bias[:, :, :, 0:SHARED].rearrange("p a b o -> p (a b) o"),
                fc2_b.rearrange("(o c n) -> o c n", o=1, c=1).to_broadcast([P, 2 * B, SHARED]))\
                .then_inc(b2_loaded, 16)
            pool.wait_ge(tr_filled, TR_W1[1, 1] + 1)
            pool.wait_ge(b2_loaded, 16)
            residual(0, 0, 0)
            residual(1, 1, 0)
            with pool.Fori(0, PAIRS) as m:
                residual(2 * m + 2, 0, m + 1)
                residual(2 * m + 3, 1, m + 1)
            residual(BLOCKS - 2, 0, BLOCKS // 2 - 1)
            residual(BLOCKS - 1, 1, BLOCKS // 2 - 1)

        @block.scalar
        def _(act):
            def transposed_hi(dst, src, n):
                act.wait_ge(tr_filled, n + 1)
                nc.scalar.activation(dst, src, ACT.Copy).then_inc(tr_hi, 1)

            def experts_hi(par, n, half, bank):
                transposed_hi(
                    w2t[:, par, :, half * HALF:(half + 1) * HALF, SHARED:OUT],
                    tr_ps[:, bank, :].rearrange("p (k b c) -> p b k c", k=HALF, b=B), n)

            def x_hi(par, n, d, bank):
                transposed_hi(xt[:, par, d, HI, :], tr_ps[:, bank, :], n)

            def w1_hi(half, d):
                n = TR_W1[half, d]
                transposed_hi(w1t[:, d, HI, half * HALF * P:(half + 1) * HALF * P],
                              w1_transposed(half, d), n)

            def chunk(i, par, j):
                n = K * i + j
                r = j // 2
                act.wait_ge(fc1_filled, n + 1)
                if j % 2 == 0 and not (isinstance(i, int) and i == 0 and r < 2):
                    act.wait_ge(h_lo, HALF * i + r - 1)
                half = slice((j % 2) * TOK, (j % 2 + 1) * TOK)
                nc.scalar.activation(gelu[:, r % 2, half], fc1_ps[:, j % FC1_BANKS, :],
                                     ACT.Gelu, bias=b1[:, j:j + 1]).then_inc(gelu_done, 1)
                if j % 2 == 1:
                    act.wait_ge(gelu_done, n + 1)
                    nc.scalar.activation(
                        ht[:, par, HI, 2 * r:2 * r + 2, :].rearrange("p k t -> p (k t)"),
                        gelu[:, r % 2, :], ACT.Copy).then_inc(h_hi, 1)

            def step(i, par, x_ahead=True):
                first = TR_FIRST + 4 * i
                for j in range(K):
                    if j in (1, 3):
                        experts_hi(1 - par, first + j // 2, j // 2, j // 2)
                    if j in (4, 6) and x_ahead:
                        x_hi(par, first + j // 2, j // 2 - 2, j // 2 - 2)
                    chunk(i + 1, 1 - par, j)

            act.dma_start(b1_in[:, :], fc1_b.rearrange("(k p) -> k p", p=P))\
                .then_inc(b1_loaded, 16)
            act.dma_start(index_sb[:, :], index.rearrange("(o n) -> o n", o=1))\
                .then_inc(index_loaded, 16)
            act.wait_ge(ident_ready, 1)
            nc.scalar.activation(gelu[:, 0, 0:1], ident[:, 0:1], ACT.Gelu).then_inc(gelu_loaded, 1)
            act.wait_ge(gelu_loaded, 1)
            for d in range(D):
                x_hi(0, TR_X0 + d, d, d)
            w1_hi(0, 0)
            w1_hi(0, 1)
            w1_hi(1, 0)
            act.wait_ge(acc_drained, 1)
            for j in range(K):
                if j == 1:
                    w1_hi(1, 1)
                if j in (2, 4):
                    x_hi(1, TR_X1 + j // 2 - 1, j // 2 - 1, j // 2 - 1)
                if j in (6, 7):
                    experts_hi(0, TR_E0 + j - 6, j - 6, j - 6)
                chunk(0, 0, j)

            step(0, 0)
            with act.Fori(0, PAIRS) as m:
                step(2 * m + 1, 1)
                step(2 * m + 2, 0)
            step(BLOCKS - 3, 1)
            step(BLOCKS - 2, 0, x_ahead=False)

        @block.vector
        def _(dve):
            def transposed_lo(dst, src, hi, n):
                dve.wait_ge(tr_hi, n + 1)
                nc.vector.tensor_tensor(dst, src, hi.bitcast(FP32), ALU.subtract)\
                    .then_inc(tr_lo, 1)

            def experts_lo(par, n, half, bank):
                ks = slice(half * HALF, (half + 1) * HALF)
                transposed_lo(
                    w2t[:, par, :, ks, OUT + SHARED:2 * OUT],
                    tr_ps[:, bank, :].rearrange("p (k b c) -> p b k c", k=HALF, b=B),
                    w2t[:, par, :, ks, SHARED:OUT], n)

            def x_lo(par, n, d, bank):
                transposed_lo(xt[:, par, d, LO, :], tr_ps[:, bank, :], xt[:, par, d, HI, :], n)

            def w1_lo(half, d):
                n = TR_W1[half, d]
                cols = slice(half * HALF * P, (half + 1) * HALF * P)
                transposed_lo(w1t[:, d, LO, cols], w1_transposed(half, d), w1t[:, d, HI, cols], n)

            def shared_split(f):
                k = 2 * (f - 1)
                src = acc_ps[:, f % 2, :].rearrange("p (k c) -> p k c", k=2)[:, :, 0:SHARED]
                hi = w2t[:, 0, 0, k:k + 2, 0:SHARED]
                dve.wait_ge(acc_filled, f + 1)
                nc.vector.tensor_copy(hi, src).then_inc(shared_hi, 1)
                dve.wait_ge(shared_hi, f)
                nc.vector.tensor_tensor(w2t[:, 0, 0, k:k + 2, OUT:OUT + SHARED], src,
                                        hi.bitcast(FP32), ALU.subtract).then_inc(acc_drained, 1)

            def pair_lo(i, par, r):
                dve.wait_ge(h_hi, HALF * i + r + 1)
                nc.vector.tensor_tensor(
                    ht[:, par, LO, 2 * r:2 * r + 2, :].rearrange("p k t -> p (k t)"),
                    gelu[:, r % 2, :],
                    ht[:, par, HI, 2 * r:2 * r + 2, :].rearrange("p k t -> p (k t)").bitcast(FP32),
                    ALU.subtract).then_inc(h_lo, 1)

            def tile_out(i, par, t):
                q = TILES * i + t
                bank = (ACC_FIRST + t) % 2
                dst = resid[:, par, t // T, (t % T) * DIM:(t % T + 1) * DIM]
                dve.wait_ge(acc_filled, ACC_FIRST + q + 1)
                if t == 0:
                    dve.wait_ge(resid_ready, i + 1)
                nc.vector.tensor_tensor(dst, acc_ps[:, bank, OUT:2 * OUT], dst, ALU.add)\
                    .then_inc(cross_added, 1)
                dve.wait_ge(cross_added, q + 1)
                nc.vector.tensor_tensor(dst, acc_ps[:, bank, 0:OUT], dst, ALU.add)\
                    .then_inc(acc_drained, 1)

            def step(i, par, x_ahead=True):
                first = TR_FIRST + 4 * i
                for j in range(K):
                    if j in (1, 3):
                        experts_lo(1 - par, first + j // 2, j // 2, j // 2)
                    if j in (4, 6) and x_ahead:
                        x_lo(par, first + j // 2, j // 2 - 2, j // 2 - 2)
                    if j % 2 == 1:
                        pair_lo(i + 1, 1 - par, j // 2)
                        tile_out(i, par, j // 2)

            dve.wait_ge(acc_filled, 1)
            nc.vector.tensor_copy(b1[:, :], acc_ps[:, 0, 0:K]).then_inc(acc_drained, 1)
            for d in range(D):
                x_lo(0, TR_X0 + d, d, d)
            w1_lo(0, 0)
            w1_lo(0, 1)
            w1_lo(1, 0)
            for j in range(K):
                if j == 1:
                    w1_lo(1, 1)
                if j in (2, 4):
                    x_lo(1, TR_X1 + j // 2 - 1, j // 2 - 1, j // 2 - 1)
                if j in (3, 4, 5, 6):
                    shared_split(j - 2)
                if j in (6, 7):
                    experts_lo(0, TR_E0 + j - 6, j - 6, j - 6)
                if j % 2 == 1:
                    pair_lo(0, 0, j // 2)
            dve.wait_ge(acc_drained, ACC_FIRST)
            for cols in (slice(0, SHARED), slice(OUT, OUT + SHARED)):
                nc.vector.tensor_copy(w2t[:, 0, 1, :, cols], w2t[:, 0, 0, :, cols].bitcast(FP32))\
                    .then_inc(row_copied, 1)

            step(0, 0)
            with dve.Fori(0, PAIRS) as m:
                step(2 * m + 1, 1)
                step(2 * m + 2, 0)
            step(BLOCKS - 3, 1)
            step(BLOCKS - 2, 0, x_ahead=False)
            for t in range(TILES):
                tile_out(BLOCKS - 1, 1, t)

        @block.tensor
        def _(pe):
            def transpose_bank(n, dst, pieces):
                if not (isinstance(n, int) and n <= TR_W1[0, 1]):
                    pe.wait_ge(tr_lo, n - 1)
                for c, piece in enumerate(pieces):
                    last = nc.tensor.transpose(dst[:, c * P:(c + 1) * P], piece, ident[:, :])
                last.then_inc(tr_filled, 1)

            def w1_bank(half, d):
                n = TR_W1[half, d]
                pe.wait_ge(w1_loaded[half], 16)
                transpose_bank(n, w1_transposed(half, d), [
                    w1_in[:, c, d * P:(d + 1) * P] for c in range(half * HALF, (half + 1) * HALF)])

            def x_bank(par, use, n, d, bank):
                if d == 0:
                    pe.wait_ge(x_loaded[par], 16 * (use + 1))
                transpose_bank(n, tr_ps[:, bank, :], [
                    x_in[:, par, t // T, (t % T) * DIM + d * P:(t % T) * DIM + (d + 1) * P]
                    for t in range(TILES)])

            def experts_bank(par, use, n, half, bank):
                if half == 0:
                    pe.wait_ge(e_loaded[par], 16 * B * (use + 1))
                transpose_bank(n, tr_ps[:, bank, :], [e_in[:, par, k * P:(k + 1) * P]
                                         for k in range(half * HALF, (half + 1) * HALF)])

            def shared_bank(f):
                if f == 1:
                    pe.wait_ge(w2_loaded, 32)
                else:
                    pe.wait_ge(acc_drained, f - 1)
                for c in range(2):
                    k = 2 * (f - 1) + c
                    ks = slice(k * P, (k + 1) * P)
                    at = c * (BANK // 2)
                    nc.tensor.transpose(acc_ps[:, f % 2, at:at + P], w2_in[:, 0, ks], ident[:, :])
                    last = nc.tensor.transpose(acc_ps[:, f % 2, at + P:at + SHARED],
                                               w2_in[0:SHARED - P, 1, ks],
                                               ident[0:SHARED - P, 0:SHARED - P])
                last.then_inc(acc_filled, 1)

            def stage2_chunk(i, par, j):
                n = K * i + j
                if not (isinstance(i, int) and i == 0 and j < FC1_BANKS):
                    pe.wait_ge(gelu_done, n - FC1_BANKS + 1)
                js = slice(j * P, (j + 1) * P)
                terms = [(d, w, v) for d in range(D) for w, v in ((HI, HI), (HI, LO), (LO, HI))]
                for at, (d, w, v) in enumerate(terms):
                    last = nc.tensor.matmul(fc1_ps[:, j % FC1_BANKS, :], w1t[:, d, w, js],
                                            xt[:, par, d, v, :],
                                            start=(at == 0), stop=(at == len(terms) - 1))
                last.then_inc(fc1_filled, 1)

            def stage3_half(i, par, t, half):
                q = TILES * i + t
                bank = (ACC_FIRST + t) % 2
                if half == 0:
                    pe.wait_ge(acc_drained, ACC_FIRST + q - 1)
                if t == 0:
                    pe.wait_ge(h_lo, HALF * i + (half + 1) * HALF // 2)
                ts = slice(t * P, (t + 1) * P)
                for k in range(half * HALF, (half + 1) * HALF):
                    nc.tensor.matmul(acc_ps[:, bank, :], ht[:, par, HI, k, ts],
                                     w2t[:, par, t // T, k, :], start=(k == 0), stop=False)
                    last = nc.tensor.matmul(acc_ps[:, bank, OUT:2 * OUT], ht[:, par, LO, k, ts],
                                            w2t[:, par, t // T, k, 0:OUT],
                                            start=False, stop=(k == K - 1))
                if half == 1:
                    last.then_inc(acc_filled, 1)

            def step(i, par, e_use, x_use, x_ahead=True):
                first = TR_FIRST + 4 * i
                peeled = isinstance(i, int) and i == 0
                pe.wait_ge(tr_lo, TR_X1 + D if peeled else first)
                for j in range(K + 1):
                    if j < K:
                        if j in (1, 3):
                            experts_bank(1 - par, e_use, first + j // 2, j // 2, j // 2)
                        if j in (4, 6) and x_ahead:
                            x_bank(par, x_use, first + j // 2, j // 2 - 2, j // 2 - 2)
                        stage2_chunk(i + 1, 1 - par, j)
                    if j == 1 and peeled:
                        pe.wait_ge(tr_lo, TR_E0 + 2)
                    if j == 2 * T + 1 and peeled:
                        pe.wait_ge(row_copied, 2)
                    if j > 0:
                        stage3_half(i, par, (j - 1) // 2, (j - 1) % 2)

            pe.wait_ge(ident_ready, 1)
            for _ in range(WARM):
                nc.tensor.matmul(fc1_ps[:, FC1_BANKS - 1, 0:P], ident[:, :], ident[:, :],
                                 start=True, stop=True)
            pe.wait_ge(b1_loaded, 16)
            nc.tensor.transpose(acc_ps[:, 0, 0:K], b1_in[:, :], ident[0:K, 0:K])\
                .then_inc(acc_filled, 1)
            for d in range(D):
                x_bank(0, 0, TR_X0 + d, d, d)
            w1_bank(0, 0)
            w1_bank(0, 1)
            w1_bank(1, 0)
            pe.wait_ge(tr_lo, TR_W1[0, 1] + 1)
            for j in range(K):
                if j == 1:
                    w1_bank(1, 1)
                if j in (2, 4):
                    x_bank(1, 0, TR_X1 + j // 2 - 1, j // 2 - 1, j // 2 - 1)
                if j in (3, 4, 5, 6):
                    shared_bank(j - 2)
                if j == 4:
                    pe.wait_ge(tr_lo, TR_W1[1, 1] + 1)
                if j in (6, 7):
                    experts_bank(0, 0, TR_E0 + j - 6, j - 6, j - 6)
                stage2_chunk(0, 0, j)

            step(0, 0, 0, 1)
            pe.wait_ge(odd_copied, 16 * 2 * B)
            with pe.Fori(0, PAIRS) as m:
                step(2 * m + 1, 1, m + 1, m + 1)
                step(2 * m + 2, 0, m + 1, m + 2)
            step(BLOCKS - 3, 1, BLOCKS // 2 - 1, BLOCKS // 2 - 1)
            step(BLOCKS - 2, 0, BLOCKS // 2 - 1, 0, x_ahead=False)
            for t in range(TILES):
                for half in range(2):
                    stage3_half(BLOCKS - 1, 1, t, half)


_INS = ["x", "itok_B_0_15", "L0_cond_fc1_w", "L0_cond_fc1_b", "L0_cond_fc2_w", "L0_cond_fc2_b",
        "L0_cond_experts_w", "L0_cond_experts_b"]


def kernel(**inputs):
    import numpy as np
    import concourse.bacc as bacc
    from concourse.bass_utils import run_bass_kernel_spmd

    nc = bacc.Bacc("TRN2", target_bir_lowering=False, num_devices=1)
    arrays, args = {}, []
    for name in _INS:
        a = np.ascontiguousarray(inputs[name])
        arrays[f"in_{name}"] = a
        args.append(nc.dram_tensor(f"in_{name}", a.shape, mybir.dt.from_np(a.dtype),
                                   kind="ExternalInput").ap())
    out = nc.dram_tensor("out", arrays["in_x"].shape, FP32, kind="ExternalOutput").ap()
    cond_mlp_residual(nc, *args, out)
    r = run_bass_kernel_spmd(nc, [arrays], core_ids=[0])
    return r.results[0]["out"]
```

```python
from contextlib import ExitStack

import concourse.bass as bass
from concourse import mybir

FP32 = mybir.dt.float32
FP32R = mybir.dt.float32r
ALU = mybir.AluOpType
ACT = mybir.ActivationFunctionType

HI, LO = 0, 1


def cond_mlp_residual(nc, x, index, fc1_w, fc1_b, fc2_w, fc2_b, experts_w, experts_b, out):
    P = 128
    ROWS, SEQ, DIM = x.shape
    HID = fc1_w.shape[0]
    SHARED = fc2_w.shape[0]
    E, PART = experts_w.shape[0], experts_w.shape[1]
    OUT = SHARED + PART
    B = 2
    T = SEQ // P
    TILES = B * T
    TOK = TILES * P
    BLOCKS = ROWS // B
    D = DIM // P
    K = HID // P
    HALF = K // 2
    BANK = 512
    FC1_BANKS = 4
    WARM = 8

    x_blocks = x.rearrange("(n b) (t p) d -> n p (b t) d", b=B, p=P)
    out_blocks = out.rearrange("(n b) (t p) d -> n p (b t) d", b=B, p=P)

    S = 32
    Q = P // S
    XJ = DIM // Q
    HJ = HID // Q
    PA = PART // S
    M = TOK // S
    x_pieces = x.rearrange("(n b) (m r) (q j) -> n q r (b m) j", b=B, r=S, q=Q)

    ctx = ExitStack()
    with ctx:
        def sbuf(name, shape, dtype=FP32):
            return ctx.enter_context(nc.sbuf_tensor(name, shape, dtype))

        def psum(name, shape):
            return ctx.enter_context(nc.psum_tensor(name, shape, FP32))

        def sem(name):
            return ctx.enter_context(nc.semaphore(name))

        w1t = sbuf("w1t", [P, D, 2, HID], FP32R)
        w2t = sbuf("w2t", [P, 2, B, K, 2 * OUT], FP32R)
        xt = sbuf("xt", [P, 2, D, 2, TOK], FP32R)
        ht = sbuf("ht", [P, 2, 2, K, TOK], FP32R)
        gelu = sbuf("gelu", [P, 2, 2 * TOK])
        x_in = sbuf("x_in", [P, 2, TILES, DIM])
        resid = sbuf("resid", [P, 2, TILES, DIM])
        pieces = sbuf("pieces", [P, 2, M * XJ + B * PA * HJ])
        x_piece = pieces[:, :, 0:M * XJ].rearrange("p n (m j) -> p n m j", m=M)
        e_piece = pieces[:, :, M * XJ:].rearrange("p n (a j) -> p n a j", j=HJ)
        SA = SHARED // S
        w2_piece = pieces[:, 1, 0:SA * HJ].rearrange("p (a j) -> p a j", a=SA)
        bias = sbuf("bias", [P, 2, B, OUT])
        ident = sbuf("ident", [P, P])
        b1_in = sbuf("b1_in", [K, P])
        b1 = sbuf("b1", [P, K])
        index_sb = sbuf("index_sb", [1, ROWS], mybir.dt.int32)
        w1_in = resid[:, :, :, :].rearrange("p a t d -> p (a t) d")

        fc1_ps = psum("fc1_ps", [P, FC1_BANKS, BANK])
        acc_ps = psum("acc_ps", [P, 2, BANK])
        tr_ps = psum("tr_ps", [P, 2, BANK])

        w1_loaded = [sem(f"w1_loaded{n}") for n in range(2)]
        w2_loaded = sem("w2_loaded")
        b1_loaded = sem("b1_loaded")
        b2_loaded = sem("b2_loaded")
        index_loaded = sem("index_loaded")
        x_piece_loaded = [sem(f"x_piece_loaded{n}") for n in range(2)]
        x_loaded = [sem(f"x_loaded{n}") for n in range(2)]
        e_loaded = [sem(f"e_loaded{n}") for n in range(2)]
        be_loaded = [sem(f"be_loaded{n}") for n in range(2)]
        stored = [sem(f"stored{n}") for n in range(2)]
        ident_zeroed = sem("ident_zeroed")
        ident_ready = sem("ident_ready")
        tr_filled = sem("tr_filled")
        sq_filled = sem("sq_filled")
        tr_hi = sem("tr_hi")
        tr_lo = sem("tr_lo")
        acc_filled = sem("acc_filled")
        shared_filled = sem("shared_filled")
        shared_hi = sem("shared_hi")
        acc_drained = sem("acc_drained")
        fc1_filled = sem("fc1_filled")
        gelu_done = sem("gelu_done")
        h_hi = sem("h_hi")
        h_lo = sem("h_lo")
        row_copied = sem("row_copied")
        odd_copied = sem("odd_copied")
        gelu_loaded = sem("gelu_loaded")
        resid_ready = sem("resid_ready")
        cross_added = sem("cross_added")

        TR_X0, TR_X1, TR_E0, TR_FIRST = 0, 6, 8, 10
        TR_W1 = {(0, 0): 2, (0, 1): 3, (1, 0): 4, (1, 1): 5}
        SQ_FIRST = TR_FIRST - TR_E0

        def w1_transposed(half, d):
            n = TR_W1[half, d]
            return fc1_ps[:, n, :] if half == 0 else tr_ps[:, n % 2, :]

        def x_at(i):
            return TR_FIRST + 4 * i

        def e_at(i, x_ahead=True):
            return x_at(i) + (D if x_ahead else 0)

        ACC_FIRST = 1 + K // 2
        PAIRS = (BLOCKS - 4) // 2

        block = ctx.enter_context(nc.Block())

        @block.sync
        def _(sp):
            def expert_numbers(row):
                return [sp.value_load(index_sb[0:1, bass.ds(row + b, 1)], min_val=0, max_val=E - 1)
                        for b in range(B)]

            def load_experts(par, experts):
                for b, e in enumerate(experts):
                    rows = experts_w[bass.ds(e, 1), :, :].rearrange(
                        "o (a r) (q j) -> q r (o a) j", r=S, q=Q)
                    for q in range(Q):
                        sp.dma_start(e_piece[S * q:S * (q + 1), par, PA * b:PA * (b + 1), :],
                                     rows[q]).then_inc(e_loaded[par], 16)
                    sp.dma_start(bias[:, par, b, SHARED:OUT],
                                 experts_b[bass.ds(e, 1), :].to_broadcast([P, PART]))\
                        .then_inc(be_loaded[par], 16)

            def load_x(i, par):
                sp.dma_start(x_in[:, par, :, :], x_blocks[i]).then_inc(x_loaded[par], 16)

            def load_x_pieces(i, par):
                for q in range(Q):
                    sp.dma_start(x_piece[S * q:S * (q + 1), par, :, :], x_pieces[i][q])\
                        .then_inc(x_piece_loaded[par], 16)

            def step(i, par, x_ahead=True, e_ahead=True):
                nxt = 1 - par
                if x_ahead:
                    if not (isinstance(i, int) and i == 0):
                        sp.wait_ge(sq_filled, SQ_FIRST + 4 * (i - 1) + D)
                    load_x_pieces(i + 3, nxt)
                if e_ahead:
                    experts = expert_numbers(B * (i + 2))
                    sp.wait_ge(sq_filled, SQ_FIRST + 4 * i)
                    load_experts(par, experts)
                if x_ahead:
                    sp.wait_ge(resid_ready, i + 2)
                    load_x(i + 3, nxt)
                for b in range(B):
                    sp.wait_ge(acc_drained, ACC_FIRST + TILES * i + T * (b + 1))
                    ts = slice(b * T, (b + 1) * T)
                    sp.dma_start(out_blocks[i][:, ts, :], resid[:, par, ts, :])\
                        .then_inc(stored[par], 16)

            load_x(0, 0)
            w1_v = fc1_w.rearrange("(q k c) d -> q c k d", q=Q, c=S)
            for half in range(2):
                ks = slice(half * HALF, (half + 1) * HALF)
                for q in range(Q):
                    sp.dma_start(w1_in[S * q:S * (q + 1), ks, :], w1_v[q][:, ks, :])\
                        .then_inc(w1_loaded[half], 16)
            w2_v = fc2_w.rearrange("(a r) (q j) -> q r a j", r=S, q=Q)
            for q in range(Q):
                sp.dma_start(w2_piece[S * q:S * (q + 1), :, :], w2_v[q]).then_inc(w2_loaded, 16)
            sp.wait_ge(index_loaded, 16)
            load_x(1, 1)
            load_experts(0, expert_numbers(0))
            load_x_pieces(2, 0)
            sp.wait_ge(shared_filled, ACC_FIRST - 1)
            load_experts(1, expert_numbers(B))
            sp.wait_ge(tr_filled, TR_X0 + 2)
            sp.wait_ge(resid_ready, 1)
            load_x(2, 0)

            step(0, 0)
            with sp.Fori(0, PAIRS) as m:
                step(2 * m + 1, 1)
                step(2 * m + 2, 0)
            step(BLOCKS - 3, 1, x_ahead=False)
            step(BLOCKS - 2, 0, x_ahead=False, e_ahead=False)
            for t in range(TILES):
                sp.wait_ge(acc_drained, ACC_FIRST + TILES * (BLOCKS - 1) + t + 1)
                sp.dma_start(out_blocks[BLOCKS - 1][:, t, :], resid[:, 1, t, :])\
                    .then_inc(stored[1], 16)
            sp.wait_ge(stored[0], 16 * B * BLOCKS // 2)
            sp.wait_ge(stored[1], 16 * (B * (BLOCKS // 2 - 1) + TILES))

        @block.gpsimd
        def _(pool):
            def residual(i, par, use):
                pool.wait_ge(x_loaded[par], 16 * (use + 1))
                pool.wait_ge(be_loaded[par], 16 * B * (use + 1))
                if not (isinstance(use, int) and use == 0):
                    pool.wait_ge(stored[par], 16 * B * use)
                nc.gpsimd.tensor_tensor(
                    resid[:, par, :, :].rearrange("p (b t) d -> p b t d", b=B),
                    x_in[:, par, :, :].rearrange("p (b t) d -> p b t d", b=B),
                    bias[:, par, :, :].unsqueeze(2).to_broadcast([P, B, T, OUT]),
                    ALU.add).then_inc(resid_ready, 1)

            nc.gpsimd.memset(ident[:, :], 0.0).then_inc(ident_zeroed, 1)
            pool.wait_ge(ident_zeroed, 1)
            nc.gpsimd.affine_select(out=ident[:, :], in_=ident[:, :], compare_op=ALU.not_equal,
                                    fill=1.0, base=0, pattern=[[-1, P]], channel_multiplier=1)\
                .then_inc(ident_ready, 1)
            pool.dma_start(
                bias[:, :, :, 0:SHARED].rearrange("p a b o -> p (a b) o"),
                fc2_b.rearrange("(o c n) -> o c n", o=1, c=1).to_broadcast([P, 2 * B, SHARED]))\
                .then_inc(b2_loaded, 16)
            pool.wait_ge(tr_filled, TR_W1[1, 1] + 1)
            pool.wait_ge(b2_loaded, 16)
            residual(0, 0, 0)
            pool.wait_ge(acc_drained, ACC_FIRST)
            for b in range(B):
                for cols in (slice(0, SHARED), slice(OUT, OUT + SHARED)):
                    pool.dma_start(w2t[:, 1, b, :, cols].bitcast(FP32),
                                   w2t[:, 0, 0, :, cols].bitcast(FP32))\
                        .then_inc(odd_copied, 16)
            residual(1, 1, 0)
            with pool.Fori(0, PAIRS) as m:
                residual(2 * m + 2, 0, m + 1)
                residual(2 * m + 3, 1, m + 1)
            residual(BLOCKS - 2, 0, BLOCKS // 2 - 1)
            residual(BLOCKS - 1, 1, BLOCKS // 2 - 1)

        @block.scalar
        def _(act):
            def transposed_hi(dst, src, n, square=True):
                if square:
                    act.wait_ge(sq_filled, n - TR_E0 + 1)
                else:
                    act.wait_ge(tr_filled, n + 1)
                nc.scalar.activation(dst, src, ACT.Copy).then_inc(tr_hi, 1)

            def experts_hi(par, n, half, bank):
                transposed_hi(
                    w2t[:, par, :, half * HALF:(half + 1) * HALF, SHARED:OUT],
                    tr_ps[:, bank, :].rearrange("p (k b c) -> p b k c", k=HALF, b=B), n)

            def x_hi(par, n, d, bank, square=True):
                transposed_hi(xt[:, par, d, HI, :], tr_ps[:, bank, :], n, square)

            def w1_hi(half, d):
                n = TR_W1[half, d]
                transposed_hi(w1t[:, d, HI, half * HALF * P:(half + 1) * HALF * P],
                              w1_transposed(half, d), n, square=False)

            def shared_part(f):
                act.wait_ge(shared_filled, f)
                k = 2 * (f - 1)
                nc.scalar.activation(
                    w2t[:, 0, 0, k:k + 2, 0:SHARED],
                    acc_ps[:, f % 2, 0:2 * SHARED].rearrange("p (k c) -> p k c", k=2),
                    ACT.Copy).then_inc(shared_hi, 1)

            def chunk(i, par, j):
                n = K * i + j
                r = j // 2
                act.wait_ge(fc1_filled, n + 1)
                if j % 2 == 0 and not (isinstance(i, int) and i == 0 and r < 2):
                    act.wait_ge(h_lo, HALF * i + r - 1)
                half = slice((j % 2) * TOK, (j % 2 + 1) * TOK)
                nc.scalar.activation(gelu[:, r % 2, half], fc1_ps[:, j % FC1_BANKS, :],
                                     ACT.Gelu, bias=b1[:, j:j + 1]).then_inc(gelu_done, 1)
                if j % 2 == 1:
                    act.wait_ge(gelu_done, n + 1)
                    nc.scalar.activation(
                        ht[:, par, HI, 2 * r:2 * r + 2, :].rearrange("p k t -> p (k t)"),
                        gelu[:, r % 2, :], ACT.Copy).then_inc(h_hi, 1)

            def step(i, par, x_ahead=True):
                for j in range(K):
                    if j in (1, 3) and x_ahead:
                        x_hi(par, x_at(i) + j // 2, j // 2, j // 2)
                    if j in (5, 7):
                        experts_hi(1 - par, e_at(i, x_ahead) + j // 2 - 2, j // 2 - 2, j // 2 - 2)
                    chunk(i + 1, 1 - par, j)

            act.dma_start(b1_in[:, :].rearrange("k (q c) -> k q c", q=Q),
                          fc1_b.rearrange("(q k c) -> k q c", q=Q, c=S))\
                .then_inc(b1_loaded, 16)
            act.dma_start(index_sb[:, :], index.rearrange("(o n) -> o n", o=1))\
                .then_inc(index_loaded, 16)
            act.wait_ge(ident_ready, 1)
            nc.scalar.activation(gelu[:, 0, 0:1], ident[:, 0:1], ACT.Gelu).then_inc(gelu_loaded, 1)
            act.wait_ge(gelu_loaded, 1)
            for d in range(D):
                x_hi(0, TR_X0 + d, d, d, square=False)
            w1_hi(0, 0)
            w1_hi(0, 1)
            act.wait_ge(acc_drained, 1)
            chunk(0, 0, 0)
            w1_hi(1, 0)
            chunk(0, 0, 1)
            w1_hi(1, 1)
            shared_part(1)
            chunk(0, 0, 2)
            shared_part(2)
            x_hi(1, TR_X1, 0, 0, square=False)
            chunk(0, 0, 3)
            x_hi(1, TR_X1 + 1, 1, 1, square=False)
            chunk(0, 0, 4)
            chunk(0, 0, 5)
            experts_hi(0, TR_E0, 0, 0)
            shared_part(3)
            chunk(0, 0, 6)
            chunk(0, 0, 7)
            shared_part(4)
            experts_hi(0, TR_E0 + 1, 1, 1)

            step(0, 0)
            with act.Fori(0, PAIRS) as m:
                step(2 * m + 1, 1)
                step(2 * m + 2, 0)
            step(BLOCKS - 3, 1)
            step(BLOCKS - 2, 0, x_ahead=False)

        @block.vector
        def _(dve):
            def transposed_lo(dst, src, hi, n):
                dve.wait_ge(tr_hi, n + 1)
                nc.vector.tensor_tensor(dst, src, hi.bitcast(FP32), ALU.subtract)\
                    .then_inc(tr_lo, 1)

            def experts_square(par, use, half, bank):
                if half == 0:
                    dve.wait_ge(e_loaded[par], 16 * B * Q * (use + 1))
                nc.vector.transpose(
                    tr_ps[:, bank, :].rearrange("p (k a c) -> p a k c", k=HALF, c=S),
                    e_piece[:, par, :, half * HALF * S:(half + 1) * HALF * S]
                    .rearrange("p a (k c) -> p a k c", c=S)).then_inc(sq_filled, 1)

            def x_square(par, use, d, bank):
                if d == 0:
                    dve.wait_ge(x_piece_loaded[par], 16 * Q * (use + 1))
                nc.vector.transpose(
                    tr_ps[:, bank, :].rearrange("p (m c) -> p m c", c=S),
                    x_piece[:, par, :, :].rearrange("p m (c d) -> p d m c", d=D)[:, d, :, :])\
                    .then_inc(sq_filled, 1)

            def experts_lo(par, n, half, bank):
                ks = slice(half * HALF, (half + 1) * HALF)
                transposed_lo(
                    w2t[:, par, :, ks, OUT + SHARED:2 * OUT],
                    tr_ps[:, bank, :].rearrange("p (k b c) -> p b k c", k=HALF, b=B),
                    w2t[:, par, :, ks, SHARED:OUT], n)

            def x_lo(par, n, d, bank):
                transposed_lo(xt[:, par, d, LO, :], tr_ps[:, bank, :], xt[:, par, d, HI, :], n)

            def w1_lo(half, d):
                n = TR_W1[half, d]
                cols = slice(half * HALF * P, (half + 1) * HALF * P)
                transposed_lo(w1t[:, d, LO, cols], w1_transposed(half, d), w1t[:, d, HI, cols], n)

            def shared_square(f):
                if f == 1:
                    dve.wait_ge(w2_loaded, 16 * Q)
                else:
                    dve.wait_ge(acc_drained, f - 1)
                k = 2 * (f - 1)
                nc.vector.transpose(
                    acc_ps[:, f % 2, 0:2 * SHARED].rearrange("p (k a c) -> p a k c", k=2, c=S),
                    w2_piece[:, :, k * S:(k + 2) * S].rearrange("p a (k c) -> p a k c", c=S))\
                    .then_inc(shared_filled, 1)

            def shared_lo(f):
                dve.wait_ge(shared_hi, f)
                k = 2 * (f - 1)
                nc.vector.tensor_tensor(
                    w2t[:, 0, 0, k:k + 2, OUT:OUT + SHARED],
                    acc_ps[:, f % 2, 0:2 * SHARED].rearrange("p (k c) -> p k c", k=2),
                    w2t[:, 0, 0, k:k + 2, 0:SHARED].bitcast(FP32), ALU.subtract)\
                    .then_inc(acc_drained, 1)

            def pair_lo(i, par, r):
                dve.wait_ge(h_hi, HALF * i + r + 1)
                nc.vector.tensor_tensor(
                    ht[:, par, LO, 2 * r:2 * r + 2, :].rearrange("p k t -> p (k t)"),
                    gelu[:, r % 2, :],
                    ht[:, par, HI, 2 * r:2 * r + 2, :].rearrange("p k t -> p (k t)").bitcast(FP32),
                    ALU.subtract).then_inc(h_lo, 1)

            def tile_out(i, par, t):
                q = TILES * i + t
                bank = (ACC_FIRST + t) % 2
                dst = resid[:, par, t, :]
                dve.wait_ge(acc_filled, 1 + q + 1)
                if t == 0:
                    dve.wait_ge(resid_ready, i + 1)
                nc.vector.tensor_tensor(dst, acc_ps[:, bank, OUT:2 * OUT], dst, ALU.add)\
                    .then_inc(cross_added, 1)
                dve.wait_ge(cross_added, q + 1)
                nc.vector.tensor_tensor(dst, acc_ps[:, bank, 0:OUT], dst, ALU.add)\
                    .then_inc(acc_drained, 1)

            def step(i, par, e_use, x_use, x_ahead=True, x_next=True):
                for r in range(HALF):
                    h = r % 2
                    pair_lo(i + 1, 1 - par, r)
                    if r == 0 and x_ahead:
                        x_square(par, None, 1, 1)
                    if r in (1, 2):
                        experts_square(1 - par, e_use, r - 1, r - 1)
                    if r == 3 and x_next:
                        x_square(1 - par, x_use, 0, 0)
                    if r >= 2:
                        experts_lo(1 - par, e_at(i, x_ahead) + h, h, h)
                    elif x_ahead:
                        x_lo(par, x_at(i) + h, h, h)
                    tile_out(i, par, r)

            dve.wait_ge(acc_filled, 1)
            nc.vector.tensor_copy(b1[:, :], acc_ps[:, 0, 0:K]).then_inc(acc_drained, 1)
            for d in range(D):
                x_lo(0, TR_X0 + d, d, d)
            w1_lo(0, 0)
            w1_lo(0, 1)
            w1_lo(1, 0)
            shared_square(1)
            shared_square(2)
            w1_lo(1, 1)
            shared_lo(1)
            pair_lo(0, 0, 0)
            shared_lo(2)
            x_lo(1, TR_X1, 0, 0)
            pair_lo(0, 0, 1)
            x_lo(1, TR_X1 + 1, 1, 1)
            dve.wait_ge(tr_lo, TR_X1 + 2)
            experts_square(0, 0, 0, 0)
            shared_square(3)
            pair_lo(0, 0, 2)
            shared_lo(3)
            experts_lo(0, TR_E0, 0, 0)
            experts_square(0, 0, 1, 1)
            shared_square(4)
            pair_lo(0, 0, 3)
            shared_lo(4)
            experts_lo(0, TR_E0 + 1, 1, 1)
            dve.wait_ge(tr_lo, TR_E0 + 2)
            x_square(0, 0, 0, 0)
            dve.wait_ge(acc_drained, ACC_FIRST)
            for cols in (slice(0, SHARED), slice(OUT, OUT + SHARED)):
                nc.vector.tensor_copy(w2t[:, 0, 1, :, cols], w2t[:, 0, 0, :, cols].bitcast(FP32))\
                    .then_inc(row_copied, 1)

            step(0, 0, 0, 0)
            with dve.Fori(0, PAIRS) as m:
                step(2 * m + 1, 1, m + 1, m + 1)
                step(2 * m + 2, 0, m + 1, m + 1)
            step(BLOCKS - 3, 1, BLOCKS // 2 - 1, None, x_next=False)
            step(BLOCKS - 2, 0, BLOCKS // 2 - 1, None, x_ahead=False, x_next=False)
            for t in range(TILES):
                tile_out(BLOCKS - 1, 1, t)

        @block.tensor
        def _(pe):
            def transpose_bank(n, dst, pieces):
                if not (isinstance(n, int) and n <= TR_W1[0, 1]):
                    pe.wait_ge(tr_lo, n - 1)
                for c, piece in enumerate(pieces):
                    last = nc.tensor.transpose(dst[:, c * P:(c + 1) * P], piece, ident[:, :])
                last.then_inc(tr_filled, 1)

            def feature_chunk(rows, d):
                return rows.rearrange("p (c d) -> p d c", d=D)[:, d, :]

            def w1_bank(half, d):
                n = TR_W1[half, d]
                pe.wait_ge(w1_loaded[half], 16 * Q)
                transpose_bank(n, w1_transposed(half, d), [
                    feature_chunk(w1_in[:, k, :], d) for k in range(half * HALF, (half + 1) * HALF)])

            def x_bank(par, n, d, bank):
                if d == 0:
                    pe.wait_ge(x_loaded[par], 16)
                transpose_bank(n, tr_ps[:, bank, :], [feature_chunk(x_in[:, par, t, :], d)
                                                      for t in range(TILES)])

            def stage2_chunk(i, par, j):
                n = K * i + j
                if not (isinstance(i, int) and i == 0 and j < FC1_BANKS):
                    pe.wait_ge(gelu_done, n - FC1_BANKS + 1)
                js = slice(j * P, (j + 1) * P)
                terms = [(d, w, v) for d in range(D) for w, v in ((HI, HI), (HI, LO), (LO, HI))]
                for at, (d, w, v) in enumerate(terms):
                    last = nc.tensor.matmul(fc1_ps[:, j % FC1_BANKS, :], w1t[:, d, w, js],
                                            xt[:, par, d, v, :],
                                            start=(at == 0), stop=(at == len(terms) - 1))
                last.then_inc(fc1_filled, 1)

            def first_chunk():
                def product(d, w, v):
                    return nc.tensor.matmul(fc1_ps[:, 0, :], w1t[:, d, w, 0:P], xt[:, 0, d, v, :],
                                            start=(d == 0 and w == v), stop=(d == D - 1 and w == LO))
                for d in range(D):
                    pe.wait_ge(tr_hi, TR_W1[0, d] + 1)
                    product(d, HI, HI)
                    pe.wait_ge(tr_lo, TR_X0 + d + 1)
                    product(d, HI, LO)
                for d in range(D):
                    pe.wait_ge(tr_lo, TR_W1[0, d] + 1)
                    last = product(d, LO, HI)
                last.then_inc(fc1_filled, 1)

            def stage3_half(i, par, t, half):
                q = TILES * i + t
                bank = (ACC_FIRST + t) % 2
                if half == 0:
                    pe.wait_ge(acc_drained, ACC_FIRST + q - 1)
                if t == 0:
                    pe.wait_ge(h_lo, HALF * i + (half + 1) * HALF // 2)
                ts = slice(t * P, (t + 1) * P)
                for k in range(half * HALF, (half + 1) * HALF):
                    nc.tensor.matmul(acc_ps[:, bank, :], ht[:, par, HI, k, ts],
                                     w2t[:, par, t // T, k, :], start=(k == 0), stop=False)
                    last = nc.tensor.matmul(acc_ps[:, bank, OUT:2 * OUT], ht[:, par, LO, k, ts],
                                            w2t[:, par, t // T, k, 0:OUT],
                                            start=False, stop=(k == K - 1))
                if half == 1:
                    last.then_inc(acc_filled, 1)

            def step(i, par):
                pe.wait_ge(tr_lo, x_at(i) - 2)
                for j in range(K + 1):
                    if j < K:
                        stage2_chunk(i + 1, 1 - par, j)
                    if j in (1, 2):
                        pe.wait_ge(tr_lo, x_at(i) - 2 + j)
                    if j == 2 * T + 1 and isinstance(i, int) and i == 0:
                        pe.wait_ge(row_copied, 2)
                    if j > 0:
                        stage3_half(i, par, (j - 1) // 2, (j - 1) % 2)

            pe.wait_ge(ident_ready, 1)
            for _ in range(WARM):
                nc.tensor.matmul(fc1_ps[:, FC1_BANKS - 1, 0:P], ident[:, :], ident[:, :],
                                 start=True, stop=True)
            pe.wait_ge(b1_loaded, 16)
            nc.tensor.transpose(acc_ps[:, 0, 0:K], b1_in[:, :], ident[0:K, 0:K])\
                .then_inc(acc_filled, 1)
            for d in range(D):
                x_bank(0, TR_X0 + d, d, d)
            w1_bank(0, 0)
            w1_bank(0, 1)
            first_chunk()
            w1_bank(1, 0)
            for j in range(1, K):
                if j == 2:
                    w1_bank(1, 1)
                if j in (3, 4):
                    x_bank(1, TR_X1 + j - 3, j - 3, j - 3)
                if j == 4:
                    pe.wait_ge(tr_lo, TR_W1[1, 1] + 1)
                stage2_chunk(0, 0, j)

            step(0, 0)
            pe.wait_ge(odd_copied, 16 * 2 * B)
            with pe.Fori(0, PAIRS) as m:
                step(2 * m + 1, 1)
                step(2 * m + 2, 0)
            step(BLOCKS - 3, 1)
            step(BLOCKS - 2, 0)
            for t in range(TILES):
                for half in range(2):
                    if t == 0:
                        pe.wait_ge(tr_lo, e_at(BLOCKS - 2, False) + half + 1)
                    stage3_half(BLOCKS - 1, 1, t, half)


_INS = ["x", "itok_B_0_15", "L0_cond_fc1_w", "L0_cond_fc1_b", "L0_cond_fc2_w", "L0_cond_fc2_b",
        "L0_cond_experts_w", "L0_cond_experts_b"]


def kernel(**inputs):
    import numpy as np
    import concourse.bacc as bacc
    from concourse.bass_utils import run_bass_kernel_spmd

    nc = bacc.Bacc("TRN2", target_bir_lowering=False, num_devices=1)
    arrays, args = {}, []
    for name in _INS:
        a = np.ascontiguousarray(inputs[name])
        arrays[f"in_{name}"] = a
        args.append(nc.dram_tensor(f"in_{name}", a.shape, mybir.dt.from_np(a.dtype),
                                   kind="ExternalInput").ap())
    out = nc.dram_tensor("out", arrays["in_x"].shape, FP32, kind="ExternalOutput").ap()
    cond_mlp_residual(nc, *args, out)
    r = run_bass_kernel_spmd(nc, [arrays], core_ids=[0])
    return r.results[0]["out"]
```
